# Optimizing a Trainium2 kernel written in Bass

```python
import numpy as np
import jax
import jax.numpy as jnp

def _softmax(x, axis=-1):
    return jax.nn.softmax(x, axis=axis)

def _gelu(x):
    return jax.nn.gelu(x, approximate=True)

def _silu(x):
    return jax.nn.silu(x)

def _sigmoid(x):
    return jax.nn.sigmoid(x)

def _layernorm(x, axis=-1, eps=1e-05):
    m = jnp.mean(x, axis=axis, keepdims=True)
    v = jnp.var(x, axis=axis, keepdims=True)
    return (x - m) / jnp.sqrt(v + eps)

def _scatter_add(tgt, idx, src, axis=0):
    return tgt.at[idx].add(src)

def _segment_sum(src, seg, n):
    return jax.ops.segment_sum(src, seg, n)
kernel_name = 'mk_rec_standalone_d1_rec_r8_0aeb01'

def setup_inputs(seed: int=0):
    np.random.seed(seed)
    _w = jnp.asarray

    def _rec_inputs():
        import jax
        import jax.numpy as jnp
        _rk = jax.random.key(seed)
        r_group = jnp.stack([jax.random.randint(jax.random.fold_in(jax.random.fold_in(_rk, 1), 0), (512,), 332, 99953, jnp.int32), jax.random.randint(jax.random.fold_in(jax.random.fold_in(_rk, 1), 1), (512,), 254, 99942, jnp.int32), jax.random.randint(jax.random.fold_in(jax.random.fold_in(_rk, 1), 2), (512,), 81, 99939, jnp.int32), jax.random.randint(jax.random.fold_in(jax.random.fold_in(_rk, 1), 3), (512,), 62, 12468, jnp.int32), jax.random.randint(jax.random.fold_in(jax.random.fold_in(_rk, 1), 4), (512,), 385, 99954, jnp.int32), jax.random.randint(jax.random.fold_in(jax.random.fold_in(_rk, 1), 5), (512,), 513, 99883, jnp.int32), jax.random.randint(jax.random.fold_in(jax.random.fold_in(_rk, 1), 6), (512,), 394, 99913, jnp.int32), jax.random.randint(jax.random.fold_in(jax.random.fold_in(_rk, 1), 7), (512,), 82, 99737, jnp.int32), jax.random.randint(jax.random.fold_in(jax.random.fold_in(_rk, 1), 8), (512,), 493, 99578, jnp.int32), jax.random.randint(jax.random.fold_in(jax.random.fold_in(_rk, 1), 9), (512,), 90, 99778, jnp.int32), jax.random.randint(jax.random.fold_in(jax.random.fold_in(_rk, 1), 10), (512,), 407, 99945, jnp.int32), jax.random.randint(jax.random.fold_in(jax.random.fold_in(_rk, 1), 11), (512,), 176, 99945, jnp.int32), jax.random.randint(jax.random.fold_in(jax.random.fold_in(_rk, 1), 12), (512,), 78, 99969, jnp.int32), jax.random.randint(jax.random.fold_in(jax.random.fold_in(_rk, 1), 13), (512,), 17, 99906, jnp.int32), jax.random.randint(jax.random.fold_in(jax.random.fold_in(_rk, 1), 14), (512,), 185, 99276, jnp.int32), jax.random.randint(jax.random.fold_in(jax.random.fold_in(_rk, 1), 15), (512,), 325, 99862, jnp.int32), jax.random.randint(jax.random.fold_in(jax.random.fold_in(_rk, 1), 16), (512,), 488, 99753, jnp.int32), jax.random.randint(jax.random.fold_in(jax.random.fold_in(_rk, 1), 17), (512,), 77, 99571, jnp.int32), jax.random.randint(jax.random.fold_in(jax.random.fold_in(_rk, 1), 18), (512,), 29, 99987, jnp.int32), jax.random.randint(jax.random.fold_in(jax.random.fold_in(_rk, 1), 19), (512,), 149, 99917, jnp.int32), jax.random.randint(jax.random.fold_in(jax.random.fold_in(_rk, 1), 20), (512,), 114, 99847, jnp.int32), jax.random.randint(jax.random.fold_in(jax.random.fold_in(_rk, 1), 21), (512,), 448, 99906, jnp.int32), jax.random.randint(jax.random.fold_in(jax.random.fold_in(_rk, 1), 22), (512,), 71, 12443, jnp.int32), jax.random.randint(jax.random.fold_in(jax.random.fold_in(_rk, 1), 23), (512,), 322, 99964, jnp.int32), jax.random.randint(jax.random.fold_in(jax.random.fold_in(_rk, 1), 24), (512,), 125, 99738, jnp.int32), jax.random.randint(jax.random.fold_in(jax.random.fold_in(_rk, 1), 25), (512,), 556, 99463, jnp.int32), jax.random.randint(jax.random.fold_in(jax.random.fold_in(_rk, 1), 26), (512,), 86, 99772, jnp.int32), jax.random.randint(jax.random.fold_in(jax.random.fold_in(_rk, 1), 27), (512,), 132, 99652, jnp.int32), jax.random.randint(jax.random.fold_in(jax.random.fold_in(_rk, 1), 28), (512,), 431, 99911, jnp.int32), jax.random.randint(jax.random.fold_in(jax.random.fold_in(_rk, 1), 29), (512,), 55, 12402, jnp.int32), jax.random.randint(jax.random.fold_in(jax.random.fold_in(_rk, 1), 30), (512,), 99, 99874, jnp.int32), jax.random.randint(jax.random.fold_in(jax.random.fold_in(_rk, 1), 31), (512,), 159, 99687, jnp.int32), jax.random.randint(jax.random.fold_in(jax.random.fold_in(_rk, 1), 32), (512,), 28, 99692, jnp.int32), jax.random.randint(jax.random.fold_in(jax.random.fold_in(_rk, 1), 33), (512,), 116, 12469, jnp.int32), jax.random.randint(jax.random.fold_in(jax.random.fold_in(_rk, 1), 34), (512,), 145, 99394, jnp.int32), jax.random.randint(jax.random.fold_in(jax.random.fold_in(_rk, 1), 35), (512,), 72, 99275, jnp.int32), jax.random.randint(jax.random.fold_in(jax.random.fold_in(_rk, 1), 36), (512,), 78, 99716, jnp.int32), jax.random.randint(jax.random.fold_in(jax.random.fold_in(_rk, 1), 37), (512,), 255, 99949, jnp.int32), jax.random.randint(jax.random.fold_in(jax.random.fold_in(_rk, 1), 38), (512,), 98, 99855, jnp.int32), jax.random.randint(jax.random.fold_in(jax.random.fold_in(_rk, 1), 39), (512,), 326, 99935, jnp.int32), jax.random.randint(jax.random.fold_in(jax.random.fold_in(_rk, 1), 40), (512,), 79, 99719, jnp.int32), jax.random.randint(jax.random.fold_in(jax.random.fold_in(_rk, 1), 41), (512,), 989, 99861, jnp.int32), jax.random.randint(jax.random.fold_in(jax.random.fold_in(_rk, 1), 42), (512,), 439, 99695, jnp.int32), jax.random.randint(jax.random.fold_in(jax.random.fold_in(_rk, 1), 43), (512,), 178, 99919, jnp.int32), jax.random.randint(jax.random.fold_in(jax.random.fold_in(_rk, 1), 44), (512,), 234, 99700, jnp.int32), jax.random.randint(jax.random.fold_in(jax.random.fold_in(_rk, 1), 45), (512,), 131, 99245, jnp.int32), jax.random.randint(jax.random.fold_in(jax.random.fold_in(_rk, 1), 46), (512,), 412, 99537, jnp.int32), jax.random.randint(jax.random.fold_in(jax.random.fold_in(_rk, 1), 47), (512,), 113, 99197, jnp.int32)], axis=1)
        return r_group
    r_group = _rec_inputs()

    def _L0_rec_setup():
        import jax, jax.numpy as jnp
        import numpy as np
        B, G, D, HID = (512, 48, 256, 30)
        NUM_USER = 12500
        key = jax.random.key(seed)
        ks = jax.random.split(key, 8)
        group = jax.random.randint(ks[0], (B, G), 0, NUM_USER)
        person_embed = jax.random.normal(ks[1], (NUM_USER + 1, D), dtype=jnp.float32) * 0.02
        first_embed = jax.random.normal(ks[2], (NUM_USER, 1), dtype=jnp.float32) * 0.02
        p = jax.random.uniform(ks[3], (D,), dtype=jnp.float32)
        W1 = jax.random.normal(ks[4], (D, HID), dtype=jnp.float32) * (1.0 / np.sqrt(D))
        b1 = jnp.zeros((HID,), dtype=jnp.float32)
        W2 = jax.random.normal(ks[5], (HID, 1), dtype=jnp.float32) * (1.0 / np.sqrt(HID))
        b2 = jnp.zeros((1,), dtype=jnp.float32)
        return {'group': group, 'person_embed': person_embed, 'first_embed': first_embed, 'p': p, 'W1': W1, 'b1': b1, 'W2': W2, 'b2': b2}
    _L0_rec_all = _L0_rec_setup()
    _L0_rec_in = {k: v for k, v in _L0_rec_all.items() if k in ('person_embed', 'first_embed', 'p', 'W1', 'b1', 'W2', 'b2')}
    del _L0_rec_all
    return {'r_group': r_group, 'L0_rec_person_embed': _L0_rec_in['person_embed'], 'L0_rec_first_embed': _L0_rec_in['first_embed'], 'L0_rec_p': _L0_rec_in['p'], 'L0_rec_W1': _L0_rec_in['W1'], 'L0_rec_b1': _L0_rec_in['b1'], 'L0_rec_W2': _L0_rec_in['W2'], 'L0_rec_b2': _L0_rec_in['b2']}

def reference(r_group, L0_rec_person_embed, L0_rec_first_embed, L0_rec_p, L0_rec_W1, L0_rec_b1, L0_rec_W2, L0_rec_b2):
    import jax
    import jax.numpy as jnp

    def _L0_rec_ref(group, person_embed, first_embed, p, W1, b1, W2, b2):
        import jax, jax.numpy as jnp
        import numpy as np
        B, G, D, HID = (512, 48, 256, 30)
        NUM_USER = 12500
        first = jnp.sum(first_embed[group][..., 0], axis=1)
        v = person_embed[group]
        iu, ju = np.triu_indices(G, k=1)
        e = v[:, iu, :] * v[:, ju, :]
        h = jax.nn.sigmoid(jnp.einsum('bpd,dh->bph', e, W1) + b1)
        a = jax.nn.sigmoid(jnp.einsum('bph,ho->bpo', h, W2) + b2)[..., 0]
        a_hat = jax.nn.softmax(a, axis=1)
        second = jnp.einsum('bpd,bp,d->b', e, a_hat, p)
        return jax.nn.sigmoid(first + second) * 2.0 - 1.0
    y = _L0_rec_ref(r_group, L0_rec_person_embed, L0_rec_first_embed, L0_rec_p, L0_rec_W1, L0_rec_b1, L0_rec_W2, L0_rec_b2)
    return y

_drawn_inputs = setup_inputs


def setup_inputs(seed=0):
    import zlib

    import numpy as np

    out = dict(_drawn_inputs(seed))
    spreads = {'L0_rec_b1': (0.0, 2.0)}
    factors = {'L0_rec_person_embed': 21.928,
     'L0_rec_p': 200.0,
     'L0_rec_W1': 64.0,
     'L0_rec_W2': 64.0,
     'L0_rec_first_embed': 8.0}
    for name, (base, spread) in spreads.items():
        noise = np.random.default_rng([zlib.crc32(name.encode()), seed]).standard_normal(out[name].shape)
        drawn = base * np.exp(spread * noise) if base else spread * noise
        out[name] = jnp.asarray(drawn.astype(out[name].dtype))
    for name, factor in factors.items():
        out[name] = (out[name] * factor).astype(out[name].dtype)
    return out
```

```python
import concourse.bass as bass
from concourse import mybir
from contextlib import ExitStack


def group_scores_program(nc, r_group, person_embed, first_embed, p, w1, b1, w2, b2, sum_rows, gate_rows, out):
    F32, I32 = mybir.dt.float32, mybir.dt.int32
    ALU, ACT, AX = mybir.AluOpType, mybir.ActivationFunctionType, mybir.AxisListType
    P = 128

    B, G = r_group.shape
    PERSONS, D = person_embed.shape
    FIRSTS = first_embed.shape[0]
    HID = w1.shape[1]
    CH = D // P
    PAIRS = G * (G - 1) // 2
    HALF = G // 2
    RING = G + HALF
    QB = 4
    CT = P // QB
    SEGS = 3
    SEG = PAIRS // SEGS
    OB = 2 * QB
    GT = OB * G // P
    STEP_QUADS = 4
    STEP_B = STEP_QUADS * QB
    STEPS = B // STEP_B
    TILES = STEP_QUADS * SEGS + SEGS
    TILE_ROWS = B * G // P
    ROWS_DVE = 17
    ROWS_POOL = HALF - 1 - ROWS_DVE
    FG = B // P
    assert D == CH * P and PAIRS == SEGS * SEG and SEG <= 512 and GT * P == OB * G and 1 + HID <= CT
    assert STEPS * STEP_B == B and HALF * 2 == G and TILE_ROWS == STEPS * 2 * GT

    with ExitStack() as ctx:
        def sb(name, shape, dt=F32):
            return ctx.enter_context(nc.sbuf_tensor(name, shape, dt))

        def psum(name, shape):
            return ctx.enter_context(nc.psum_tensor(name, shape, F32))

        def sem(name):
            return ctx.enter_context(nc.semaphore(name))

        ident = sb("ident", [P, P])
        weights = sb("weights", [P, CH, CT])
        bias1 = sb("bias1", [P, 1])
        gate_w = sb("gate_w", [P, CT])
        bias2 = sb("bias2", [P, 1])
        GATE_STRIDE = CT // QB
        IH = TILE_ROWS // 2
        raw_rows = sb("raw_rows", [IH, 2, P], I32)
        rows_f = sb("rows_f", [IH, 2, P])
        rows_neg = sb("rows_neg", [IH, 2, P])
        person_idx = sb("person_idx", [P, TILE_ROWS + GT], I32)
        raw_first = sb("raw_first", [P, FG * G], I32)
        first_f = sb("first_f", [P, FG * G])
        first_neg = sb("first_neg", [P, FG * G])
        first_idx = sb("first_idx", [P, FG * G], I32)
        near_persons = sb("near_persons", [P, 2, GT], I32)
        near_firsts = sb("near_firsts", [P, 2, GT], I32)
        first_now = sb("first_now", [P, 2, GT])
        first_vals = sb("first_vals", [P, FG * G])
        gathered = sb("gathered", [P, 2, GT, D])
        ringed = sb("ringed", [P, 2, CH, OB, RING])
        pairs = sb("pairs", [P, 2, CH, QB, PAIRS])
        hidden = sb("hidden", [P, STEP_QUADS, PAIRS])
        sums = sb("sums", [P, 2, PAIRS])
        gates = sb("gates", [P, PAIRS])
        all_sums = sb("all_sums", [P, FG, PAIRS])
        all_gates = sb("all_gates", [P, FG, PAIRS])
        stat = sb("stat", [P, 8, FG])
        NMAX, DEN, RDEN, NUM, FIRST, TOTAL, SIG, RES = range(8)

        members = psum("members", [P, 2, CH, 512])
        score = psum("score", [P, SEGS, 512])

        s_rows, s_frows, s_const = sem("s_rows"), sem("s_frows"), sem("s_const")
        s_zero, s_ident0, s_ident = sem("s_zero"), sem("s_ident0"), sem("s_ident")
        s_prep, s_rows_ready, s_rowsT, s_idx, s_fidx = (sem("s_prep"), sem("s_rows_ready"), sem("s_rowsT"),
                                                        sem("s_idx"), sem("s_fidx"))
        s_gath = [sem("s_gath0"), sem("s_gath1")]
        s_first = [sem("s_first0"), sem("s_first1")]
        s_near = sem("s_near")
        s_kept = sem("s_kept")
        s_members = sem("s_members")
        s_ringed = sem("s_ringed")
        s_edve = sem("s_edve")
        s_epool = sem("s_epool")
        s_tile = sem("s_tile")
        s_read = sem("s_read")
        s_sumout = [sem("s_sumout0"), sem("s_sumout1")]
        s_gateout = sem("s_gateout")
        s_back = [sem("s_back_gates"), sem("s_back_sums")]
        s_max, s_exp, s_fin, s_sig, s_chain, s_res, s_out = (sem("s_max"), sem("s_exp"), sem("s_fin"), sem("s_sig"),
                                                             sem("s_chain"), sem("s_res"), sem("s_out"))

        def shifted(slot, c, b0, nb, k0, nk, ni):
            a = ringed[:, slot, c, b0:b0 + 1, k0:k0 + 1]
            return bass.AP(a.tensor, a.offset, [a.ap[0], [RING, nb], [1, nk], [1, ni]])

        def repeated(t, nk, ni):
            return bass.AP(t.tensor, t.offset, [t.ap[0], t.ap[1], [0, nk], [1, ni]])

        def rows_of(slot, c, k0, nk):
            return pairs[:, slot, c, :, (k0 - 1) * G:(k0 - 1 + nk) * G].rearrange("p b (k i) -> p b k i", i=G)

        def steps(eng, body):
            body(0)
            with eng.Fori(1, STEPS - 1) as n:
                body(n)
            body(STEPS - 1)

        def is_first(n):
            return isinstance(n, int) and n == 0

        def is_last(n):
            return isinstance(n, int) and n == STEPS - 1

        def tiles_before(n, q):
            if q < 0:
                return TILES * (n - 1) + SEGS * (q + STEP_QUADS)
            return TILES * n + SEGS * q

        with nc.Block() as block:

            @block.sync
            def _(sp):
                sp.dma_start(raw_rows[:, :, :],
                             r_group.rearrange("b i -> (b i)").rearrange("(h n r) -> n h r", h=2, r=P)).then_inc(s_rows, 16)
                sp.dma_start(raw_first[:, :], r_group.rearrange("(p g) i -> p (g i)", g=FG)).then_inc(s_frows, 16)
                sp.wait_ge(s_zero, 1)
                sp.dma_start(weights[:, :, 1:1 + HID], w1.rearrange("(c p) h -> p c h", p=P)).then_inc(s_const, 16)
                sp.dma_start(weights[:, :, 0:1], p.rearrange("(c p a) -> p c a", p=P, a=1),
                             allow_slow_non_contiguous=True).then_inc(s_const, 16)
                for t in range(QB):
                    sp.dma_start(bias1[CT * t + 1:CT * t + 1 + HID, :], b1.rearrange("(h a) -> h a", a=1)).then_inc(s_const, 16)
                    sp.dma_start(gate_w[CT * t + 1:CT * t + 1 + HID, GATE_STRIDE * t:GATE_STRIDE * t + 1],
                                 w2).then_inc(s_const, 16)
                sp.dma_start(bias2[:, :], b2.rearrange("(a n) -> a n", a=1).broadcast_to([P, 1])).then_inc(s_const, 16)

                def step(n):
                    for q in range(STEP_QUADS):
                        sp.wait_ge(s_read, tiles_before(n, q + 1))
                        sp.dma_start(sum_rows[bass.ds(STEP_B * n + QB * q, QB), :],
                                     sums[0:P:CT, q % 2, :]).then_inc(s_sumout[q % 2], 16)
                    sp.wait_ge(s_read, TILES * n + TILES)
                    sp.dma_start(gate_rows[bass.ds(STEP_B * n, STEP_B), :],
                                 gates[0:P:GATE_STRIDE, :]).then_inc(s_gateout, 16)

                steps(sp, step)
                sp.wait_ge(s_gateout, 16 * STEPS)
                sp.dma_start(all_gates[:, :, :], gate_rows.rearrange("(p g) w -> p g w", g=FG)).then_inc(s_back[0], 16)
                for s in s_sumout:
                    sp.wait_ge(s, 16 * STEPS * STEP_QUADS // 2)
                sp.dma_start(all_sums[:, :, :], sum_rows.rearrange("(p g) w -> p g w", g=FG)).then_inc(s_back[1], 16)
                sp.wait_ge(s_res, 1)
                sp.dma_start(out.rearrange("(p g) -> p g", g=FG), stat[:, RES, :]).then_inc(s_out, 16)
                sp.wait_ge(s_out, 16)

            @block.gpsimd
            def _(pool):
                nc.gpsimd.memset(ident[:, :], 0.0).then_inc(s_ident0, 1)
                pool.wait_ge(s_ident0, 1)
                nc.gpsimd.affine_select(out=ident[:, :], in_=ident[:, :], compare_op=ALU.not_equal, fill=1.0,
                                        base=0, pattern=[[-1, P]], channel_multiplier=1).then_inc(s_ident, 1)

                def gather(slot):
                    for j in range(GT):
                        nc.gpsimd.indirect_dma_start(
                            gathered[:, slot, j, :], None, person_embed[:, :],
                            bass.IndirectOffsetOnAxis(ap=near_persons[:, slot, j:j + 1], axis=0)).then_inc(s_gath[slot], 16)

                def gather_first(slot):
                    for j in range(GT):
                        nc.gpsimd.indirect_dma_start(
                            first_now[:, slot, j:j + 1], None, first_embed[:, :],
                            bass.IndirectOffsetOnAxis(ap=near_firsts[:, slot, j:j + 1], axis=0)).then_inc(s_first[slot], 16)

                pool.wait_ge(s_near, 1)
                gather(0)
                gather(1)

                def step(n):
                    for q in range(STEP_QUADS):
                        slot, b0 = q // 2, QB * (q % 2)
                        if q % 2 == 0:
                            pool.wait_ge(s_ringed, 2 * n + slot + 1)
                        if not (is_first(n) and q < 2):
                            pool.wait_ge(s_tile, tiles_before(n, q - 1))
                        for c in range(CH):
                            nc.gpsimd.tensor_tensor(rows_of(q % 2, c, ROWS_DVE + 1, ROWS_POOL),
                                                    repeated(ringed[:, slot, c, b0:b0 + QB, 0:G], ROWS_POOL, G),
                                                    shifted(slot, c, b0, QB, ROWS_DVE + 1, ROWS_POOL, G), ALU.mult)
                        nc.gpsimd.tensor_tensor(pairs[:, q % 2, :, :, PAIRS - HALF:PAIRS],
                                                ringed[:, slot, :, b0:b0 + QB, 0:HALF],
                                                ringed[:, slot, :, b0:b0 + QB, HALF:G], ALU.mult).then_inc(s_epool, 1)
                        if q % 2 == 0:
                            if not is_last(n):
                                gather(slot)
                            gather_first(slot)

                steps(pool, step)

            @block.vector
            def _(dve):
                chain = [0]

                def link(ins):
                    chain[0] += 1
                    ins.then_inc(s_chain, 1)
                    dve.wait_ge(s_chain, chain[0])

                nc.vector.memset(bias1[:, :], 0.0)
                nc.vector.memset(gate_w[:, :], 0.0)
                nc.vector.memset(weights[:, :, :], 0.0).then_inc(s_zero, 1)

                def bounded(dst, neg, raw, size):
                    link(nc.vector.tensor_copy(dst, raw))
                    link(nc.vector.tensor_scalar(dst, dst, float(size - 1), float(-size), ALU.min, ALU.max))
                    link(nc.vector.tensor_scalar(neg, dst, 0.0, float(size), ALU.is_lt, ALU.mult))
                    return nc.vector.tensor_tensor(dst, dst, neg, ALU.add)

                dve.wait_ge(s_rows, 16)
                bounded(rows_f[:, :, :], rows_neg[:, :, :], raw_rows[:, :, :], PERSONS).then_inc(s_rows_ready, 1)
                dve.wait_ge(s_rowsT, 1)
                nc.vector.memset(person_idx[:, TILE_ROWS:], 0)
                nc.vector.tensor_copy(person_idx[:, 0:TILE_ROWS], members[:, 0, 0, 0:TILE_ROWS]).then_inc(s_idx, 1)
                dve.wait_ge(s_frows, 16)
                link(bounded(first_f[:, :], first_neg[:, :], raw_first[:, :], FIRSTS))
                nc.vector.tensor_copy(first_idx[:, :], first_f[:, :]).then_inc(s_fidx, 1)

                def step(n):
                    for q in range(STEP_QUADS):
                        slot, b0 = q // 2, QB * (q % 2)
                        if q % 2 == 0:
                            dve.wait_ge(s_ringed, 2 * n + slot + 1)
                        if not (is_first(n) and q < 2):
                            dve.wait_ge(s_tile, tiles_before(n, q - 1))
                        for c in range(CH):
                            here = members[:, slot, c, b0 * G:(b0 + QB) * G].rearrange("p (b i) -> p b i", i=G)
                            nc.vector.tensor_tensor(rows_of(q % 2, c, 1, ROWS_DVE),
                                                    repeated(here, ROWS_DVE, G),
                                                    shifted(slot, c, b0, QB, 1, ROWS_DVE, G), ALU.mult).then_inc(s_edve, 1)

                steps(dve, step)

                dve.wait_ge(s_kept, 2 * STEPS)
                nc.vector.tensor_reduce(out=stat[:, FIRST, :], in_=first_vals[:, :].rearrange("p (g i) -> p g i", i=G),
                                        axis=AX.X, op=ALU.add)
                dve.wait_ge(s_back[0], 16)
                link(nc.vector.tensor_reduce(out=stat[:, NUM, :], in_=all_gates[:, :, :], axis=AX.X, op=ALU.max))
                nc.vector.tensor_scalar(stat[:, NMAX, :], stat[:, NUM, :], -1.0, None, ALU.mult).then_inc(s_max, 1)
                dve.wait_ge(s_back[1], 16)
                for g in range(FG):
                    dve.wait_ge(s_exp, g + 1)
                    link(nc.vector.tensor_tensor_reduce(out=all_sums[:, g, :], in0=all_sums[:, g, :], in1=all_gates[:, g, :],
                                                        scale=1.0, scalar=0.0, op0=ALU.mult, op1=ALU.add,
                                                        accum_out=stat[:, NUM, g:g + 1]))
                link(nc.vector.reciprocal(stat[:, RDEN, :], stat[:, DEN, :]))
                link(nc.vector.tensor_tensor(stat[:, TOTAL, :], stat[:, NUM, :], stat[:, RDEN, :], ALU.mult))
                nc.vector.tensor_tensor(stat[:, TOTAL, :], stat[:, TOTAL, :], stat[:, FIRST, :], ALU.add).then_inc(s_fin, 1)
                dve.wait_ge(s_sig, 1)
                nc.vector.tensor_scalar(stat[:, RES, :], stat[:, SIG, :], 2.0, -1.0, ALU.mult, ALU.add).then_inc(s_res, 1)

            @block.tensor
            def _(pe):
                pe.wait_ge(s_ident, 1)
                pe.wait_ge(s_rows_ready, 1)
                for h in range(2):
                    last = nc.tensor.transpose(members[:, 0, 0, h * IH:(h + 1) * IH], rows_f[:, h, :], ident[0:IH, 0:IH])
                last.then_inc(s_rowsT, 1)

                def transpose_oct(n, slot, rounds):
                    pe.wait_ge(s_gath[slot], 16 * GT * (rounds + 1))
                    if not (isinstance(rounds, int) and rounds == 0):
                        pe.wait_ge(s_edve, CH * 4 * rounds - (0 if slot else 2 * CH))
                    for j in range(GT):
                        for c in range(CH):
                            last = nc.tensor.transpose(members[:, slot, c, j * P:(j + 1) * P],
                                                       gathered[:, slot, j, c * P:(c + 1) * P], ident[:, :])
                    last.then_inc(s_members, 1)

                pe.wait_ge(s_idx, 1)
                transpose_oct(0, 0, 0)
                pe.wait_ge(s_const, 16 * (2 * QB + 3))

                def step(n):
                    transpose_oct(n, 1, n)
                    for q in range(STEP_QUADS):
                        if q == 2 and not is_last(n):
                            transpose_oct(n + 1, 0, n + 1)
                        pe.wait_ge(s_edve, CH * (STEP_QUADS * n + q + 1))
                        pe.wait_ge(s_epool, STEP_QUADS * n + q + 1)
                        for s in range(SEGS):
                            if not (is_first(n) and q == 0):
                                pe.wait_ge(s_read, tiles_before(n, q - 1) + s + 1 if q else TILES * n - SEGS + s + 1)
                            for c in range(CH):
                                for t in range(QB):
                                    last = nc.tensor.matmul(score[CT * t:CT * (t + 1), s, 0:SEG], weights[:, c, :],
                                                            pairs[:, q % 2, c, t, s * SEG:(s + 1) * SEG],
                                                            start=(c == 0), stop=(c == CH - 1))
                            last.then_inc(s_tile, 1)
                    for s in range(SEGS):
                        pe.wait_ge(s_read, TILES * n + SEGS * STEP_QUADS - SEGS + s + 1)
                        for q in range(STEP_QUADS):
                            last = nc.tensor.matmul(score[CT * q:CT * (q + 1), s, 0:SEG], gate_w[:, :],
                                                    hidden[:, q, s * SEG:(s + 1) * SEG], start=True, stop=True)
                        last.then_inc(s_tile, 1)

                steps(pe, step)

            @block.scalar
            def _(act):
                def next_persons(slot, o):
                    return nc.scalar.copy(near_persons[:, slot, :], person_idx[:, bass.ds(GT * o, GT)])

                def keep_firsts(slot, o, rounds):
                    act.wait_ge(s_first[slot], 16 * GT * rounds)
                    nc.scalar.copy(first_vals[:, bass.ds(GT * o, GT)], first_now[:, slot, :]).then_inc(s_kept, 1)

                def ring_oct(slot, o, rounds):
                    start = isinstance(rounds, int) and rounds == 0
                    if not start:
                        keep_firsts(slot, o - 2, rounds)
                    nc.scalar.copy(near_firsts[:, slot, :], first_idx[:, bass.ds(GT * o, GT)])
                    act.wait_ge(s_members, o + 1)
                    if not (slot == 1 and is_last(rounds)):
                        next_persons(slot, o + 2)
                    if not start:
                        act.wait_ge(s_edve, 2 * CH * (o - 1))
                        act.wait_ge(s_epool, 2 * (o - 1))
                    for c in range(CH):
                        here = members[:, slot, c, 0:OB * G].rearrange("p (b i) -> p b i", i=G)
                        nc.scalar.copy(ringed[:, slot, c, :, 0:G], here)
                        last = nc.scalar.copy(ringed[:, slot, c, :, G:RING], here[:, :, 0:HALF])
                    last.then_inc(s_ringed, 1)

                act.wait_ge(s_idx, 1)
                next_persons(0, 0)
                next_persons(1, 1).then_inc(s_near, 1)
                act.wait_ge(s_fidx, 1)
                ring_oct(0, 0, 0)
                act.wait_ge(s_const, 16 * (2 * QB + 3))

                def step(n):
                    ring_oct(1, 2 * n + 1, n)
                    for q in range(STEP_QUADS):
                        if q == 2 and not is_last(n):
                            ring_oct(0, 2 * n + 2, n + 1)
                        if not (is_first(n) and q < 2):
                            act.wait_ge(s_sumout[q % 2], 32 * n + 16 * (q // 2))
                        for s in range(SEGS):
                            act.wait_ge(s_tile, tiles_before(n, q) + s + 1)
                            seg = slice(s * SEG, (s + 1) * SEG)
                            nc.scalar.activation(hidden[:, q, seg], score[:, s, 0:SEG], ACT.Sigmoid, bias=bias1[:, :])
                            nc.scalar.copy(sums[:, q % 2, seg], score[:, s, 0:SEG]).then_inc(s_read, 1)
                    if not is_first(n):
                        act.wait_ge(s_gateout, 16 * n)
                    for s in range(SEGS):
                        act.wait_ge(s_tile, TILES * n + SEGS * STEP_QUADS + s + 1)
                        nc.scalar.activation(gates[:, s * SEG:(s + 1) * SEG], score[:, s, 0:SEG], ACT.Sigmoid,
                                             bias=bias2[:, :]).then_inc(s_read, 1)

                steps(act, step)
                for slot in range(2):
                    keep_firsts(slot, 2 * STEPS - 2 + slot, STEPS)
                act.wait_ge(s_max, 1)
                for g in range(FG):
                    nc.scalar.activation(all_gates[:, g, :], all_gates[:, g, :], ACT.Exp, bias=stat[:, NMAX, g:g + 1],
                                         accum_out=stat[:, DEN, g:g + 1]).then_inc(s_exp, 1)
                act.wait_ge(s_fin, 1)
                nc.scalar.activation(stat[:, SIG, :], stat[:, TOTAL, :], ACT.Sigmoid).then_inc(s_sig, 1)


_INS = ['r_group', 'L0_rec_person_embed', 'L0_rec_first_embed', 'L0_rec_p', 'L0_rec_W1', 'L0_rec_b1', 'L0_rec_W2', 'L0_rec_b2']


def kernel(**inputs):
    import numpy as _np
    import concourse.bacc as _bacc
    from concourse import mybir as _mybir
    from concourse.bass_utils import run_bass_kernel_spmd as _run

    nc = _bacc.Bacc("TRN2", target_bir_lowering=False, num_devices=1)
    arrays, args = {}, []
    for name in _INS:
        a = _np.ascontiguousarray(inputs[name])
        arrays[f"in_{name}_dram"] = a
        args.append(nc.dram_tensor(f"in_{name}_dram", a.shape, _mybir.dt.from_np(a.dtype), kind="ExternalInput").ap())
    groups, members = inputs['r_group'].shape
    scratch = (groups, members * (members - 1) // 2)
    for name in ("sum_rows", "gate_rows"):
        args.append(nc.dram_tensor(name, scratch, _mybir.dt.float32, kind="Internal").ap())
    args.append(nc.dram_tensor("out_0_dram", (groups,), _mybir.dt.float32, kind="ExternalOutput").ap())
    group_scores_program(nc, *args)
    r = _run(nc, [arrays], core_ids=[0])
    return r.results[0]["out_0_dram"]
```

```python
import concourse.bass as bass
from concourse import mybir
from contextlib import ExitStack


def group_scores_program(nc, r_group, person_embed, first_embed, p, w1, b1, w2, b2, sum_rows, gate_rows, out):
    F32, I32 = mybir.dt.float32, mybir.dt.int32
    ALU, ACT, AX = mybir.AluOpType, mybir.ActivationFunctionType, mybir.AxisListType
    P = 128

    B, G = r_group.shape
    PERSONS, D = person_embed.shape
    FIRSTS = first_embed.shape[0]
    HID = w1.shape[1]
    CH = D // P
    PAIRS = G * (G - 1) // 2
    ROW = G - 1
    ROWS = G // 2 - 1
    RING = G + ROWS
    QB = 4
    CT = P // QB
    SEGS = 3
    SEG = PAIRS // SEGS
    OB = 2 * QB
    GT = OB * G // P
    STEP_QUADS = 4
    STEP_B = STEP_QUADS * QB
    STEPS = B // STEP_B
    TILES = STEP_QUADS * SEGS + SEGS
    TILE_ROWS = B * G // P
    ROWS_DVE = 18
    ROWS_POOL = ROWS - ROWS_DVE
    FG = B // P
    assert D == CH * P and PAIRS == SEGS * SEG and SEG <= 512 and GT * P == OB * G and 1 + HID <= CT
    assert STEPS * STEP_B == B and G % 2 == 0 and (ROWS + 1) * ROW == PAIRS and TILE_ROWS == STEPS * 2 * GT

    with ExitStack() as ctx:
        def sb(name, shape, dt=F32):
            return ctx.enter_context(nc.sbuf_tensor(name, shape, dt))

        def psum(name, shape):
            return ctx.enter_context(nc.psum_tensor(name, shape, F32))

        def sem(name):
            return ctx.enter_context(nc.semaphore(name))

        ident = sb("ident", [P, P])
        weights = sb("weights", [P, CH, CT])
        bias1 = sb("bias1", [P, 1])
        gate_w = sb("gate_w", [P, CT])
        bias2 = sb("bias2", [P, 1])
        GATE_STRIDE = CT // QB
        IH = TILE_ROWS // 2
        raw_rows = sb("raw_rows", [IH, 2, P], I32)
        rows_f = sb("rows_f", [IH, 2, P])
        rows_neg = sb("rows_neg", [IH, 2, P])
        person_idx = sb("person_idx", [P, TILE_ROWS + GT], I32)
        raw_first = sb("raw_first", [P, FG * G], I32)
        first_f = sb("first_f", [P, FG * G])
        first_neg = sb("first_neg", [P, FG * G])
        first_idx = sb("first_idx", [P, FG * G], I32)
        near_persons = sb("near_persons", [P, 2, GT], I32)
        near_firsts = sb("near_firsts", [P, 2, GT], I32)
        first_now = sb("first_now", [P, 2, GT])
        first_vals = sb("first_vals", [P, FG * G])
        gathered = sb("gathered", [P, 2, GT, D])
        ringed = sb("ringed", [P, 2, CH, OB, RING])
        pairs = sb("pairs", [P, 2, CH, QB, PAIRS])
        hidden = sb("hidden", [P, STEP_QUADS, PAIRS])
        sums = sb("sums", [P, 2, PAIRS])
        gates = sb("gates", [P, PAIRS])
        all_sums = sb("all_sums", [P, FG, PAIRS])
        all_gates = sb("all_gates", [P, FG, PAIRS])
        stat = sb("stat", [P, 8, FG])
        MAX, NMAX, DEN, RDEN, NUM, FIRST, TOTAL, SIG = range(8)
        result = sb("result", [FG, P])

        members = psum("members", [P, 2, CH, 512])
        score = psum("score", [P, SEGS, 512])

        s_rows, s_frows, s_const = sem("s_rows"), sem("s_frows"), sem("s_const")
        s_zero, s_ident0, s_ident = sem("s_zero"), sem("s_ident0"), sem("s_ident")
        s_prep, s_rows_ready, s_rowsT, s_idx, s_fidx = (sem("s_prep"), sem("s_rows_ready"), sem("s_rowsT"),
                                                        sem("s_idx"), sem("s_fidx"))
        s_gath = [sem("s_gath0"), sem("s_gath1")]
        s_first = [sem("s_first0"), sem("s_first1")]
        s_near = sem("s_near")
        s_kept = sem("s_kept")
        s_members = sem("s_members")
        s_ringed = sem("s_ringed")
        s_edve = sem("s_edve")
        s_eact = sem("s_eact")
        s_epool = sem("s_epool")
        s_tile = sem("s_tile")
        s_read = sem("s_read")
        s_sumout = [sem("s_sumout0"), sem("s_sumout1")]
        s_gateout = sem("s_gateout")
        s_early = sem("s_early")
        s_late = [sem("s_late_gates"), sem("s_late_sums")]
        s_max, s_exp, s_fin, s_sig, s_chain, s_sigT, s_res, s_out = (sem("s_max"), sem("s_exp"), sem("s_fin"), sem("s_sig"),
                                                             sem("s_chain"), sem("s_sigT"), sem("s_res"), sem("s_out"))

        def shifted(slot, c, b0, k0, nk):
            a = ringed[:, slot, c, b0:b0 + 1, 1 + k0:2 + k0]
            return bass.AP(a.tensor, a.offset, [a.ap[0], [RING, QB], [1, nk], [1, ROW]])

        def repeated(t, nk):
            return bass.AP(t.tensor, t.offset, [t.ap[0], t.ap[1], [0, nk], [1, ROW]])

        def rows_of(slot, c, k0, nk):
            return pairs[:, slot, c, :, (k0 - 1) * ROW:(k0 - 1 + nk) * ROW].rearrange("p b (k i) -> p b k i", i=ROW)

        def steps(eng, body, before_last=None):
            body(0)
            with eng.Fori(1, STEPS - 1) as n:
                body(n)
            if before_last:
                before_last()
            body(STEPS - 1)

        def is_first(n):
            return isinstance(n, int) and n == 0

        def is_last(n):
            return isinstance(n, int) and n == STEPS - 1

        def tiles_before(n, q):
            if q < 0:
                return TILES * (n - 1) + SEGS * (q + STEP_QUADS)
            return TILES * n + SEGS * q

        with nc.Block() as block:

            @block.sync
            def _(sp):
                sp.dma_start(raw_rows[:, :, :],
                             r_group.rearrange("b i -> (b i)").rearrange("(h n r) -> n h r", h=2, r=P)).then_inc(s_rows, 16)
                sp.dma_start(raw_first[:, :].rearrange("p (g i) -> p g i", i=G), r_group.rearrange("(g p) i -> p g i", g=FG)).then_inc(s_frows, 16)
                sp.wait_ge(s_zero, 1)
                sp.dma_start(weights[:, :, 1:1 + HID], w1.rearrange("(c p) h -> p c h", p=P)).then_inc(s_const, 16)
                sp.dma_start(weights[:, :, 0:1], p.rearrange("(c p a) -> p c a", p=P, a=1),
                             allow_slow_non_contiguous=True).then_inc(s_const, 16)
                for t in range(QB):
                    sp.dma_start(bias1[CT * t + 1:CT * t + 1 + HID, :], b1.rearrange("(h a) -> h a", a=1)).then_inc(s_const, 16)
                    sp.dma_start(gate_w[CT * t + 1:CT * t + 1 + HID, GATE_STRIDE * t:GATE_STRIDE * t + 1],
                                 w2).then_inc(s_const, 16)
                sp.dma_start(bias2[:, :], b2.rearrange("(a n) -> a n", a=1).broadcast_to([P, 1])).then_inc(s_const, 16)

                def step(n):
                    for q in range(STEP_QUADS):
                        sp.wait_ge(s_read, tiles_before(n, q + 1))
                        sp.dma_start(sum_rows[bass.ds(STEP_B * n + QB * q, QB), :],
                                     sums[0:P:CT, q % 2, :]).then_inc(s_sumout[q % 2], 16)
                    sp.wait_ge(s_read, TILES * n + TILES)
                    sp.dma_start(gate_rows[bass.ds(STEP_B * n, STEP_B), :],
                                 gates[0:P:GATE_STRIDE, :]).then_inc(s_gateout, 16)

                def blocks(rows, g0, g1):
                    return rows[P * g0:P * g1, :].rearrange("(g p) w -> p g w", p=P)

                def fetch_early():
                    steps_done = (FG - 1) * P // STEP_B
                    sp.wait_ge(s_gateout, 16 * steps_done)
                    for s in s_sumout:
                        sp.wait_ge(s, 16 * steps_done * STEP_QUADS // 2)
                    sp.dma_start(all_gates[:, 0:FG - 1, :], blocks(gate_rows, 0, FG - 1)).then_inc(s_early, 16)
                    sp.dma_start(all_sums[:, 0:FG - 1, :], blocks(sum_rows, 0, FG - 1)).then_inc(s_early, 16)

                steps(sp, step, fetch_early)
                for s in s_sumout:
                    sp.wait_ge(s, 16 * STEPS * STEP_QUADS // 2)
                sp.dma_start(all_sums[:, FG - 1:FG, :], blocks(sum_rows, FG - 1, FG)).then_inc(s_late[1], 16)
                sp.wait_ge(s_gateout, 16 * STEPS)
                sp.dma_start(all_gates[:, FG - 1:FG, :], blocks(gate_rows, FG - 1, FG)).then_inc(s_late[0], 16)
                sp.wait_ge(s_res, 1)
                sp.dma_start(out.rearrange("(g p) -> g p", p=P), result[:, :]).then_inc(s_out, 16)
                sp.wait_ge(s_out, 16)

            @block.gpsimd
            def _(pool):
                nc.gpsimd.memset(ident[:, :], 0.0).then_inc(s_ident0, 1)
                pool.wait_ge(s_ident0, 1)
                nc.gpsimd.affine_select(out=ident[:, :], in_=ident[:, :], compare_op=ALU.not_equal, fill=1.0,
                                        base=0, pattern=[[-1, P]], channel_multiplier=1).then_inc(s_ident, 1)

                def gather(slot):
                    for j in range(GT):
                        nc.gpsimd.indirect_dma_start(
                            gathered[:, slot, j, :], None, person_embed[:, :],
                            bass.IndirectOffsetOnAxis(ap=near_persons[:, slot, j:j + 1], axis=0)).then_inc(s_gath[slot], 16)

                def gather_first(slot):
                    for j in range(GT):
                        nc.gpsimd.indirect_dma_start(
                            first_now[:, slot, j:j + 1], None, first_embed[:, :],
                            bass.IndirectOffsetOnAxis(ap=near_firsts[:, slot, j:j + 1], axis=0)).then_inc(s_first[slot], 16)

                pool.wait_ge(s_near, 1)
                gather(0)
                gather(1)

                def step(n):
                    for q in range(STEP_QUADS):
                        slot, b0 = q // 2, QB * (q % 2)
                        if q % 2 == 0:
                            pool.wait_ge(s_ringed, 2 * n + slot + 1)
                        if not (is_first(n) and q < 2):
                            pool.wait_ge(s_tile, tiles_before(n, q - 1))
                        for c in range(CH):
                            last = nc.gpsimd.tensor_tensor(rows_of(q % 2, c, ROWS_DVE + 1, ROWS_POOL),
                                                    repeated(ringed[:, slot, c, b0:b0 + QB, 1:G], ROWS_POOL),
                                                                  shifted(slot, c, b0, ROWS_DVE + 1, ROWS_POOL), ALU.mult)
                        last.then_inc(s_epool, 1)
                        if q % 2 == 0:
                            if not is_last(n):
                                gather(slot)
                            gather_first(slot)

                steps(pool, step)

            @block.vector
            def _(dve):
                chain = [0]

                def link(ins):
                    chain[0] += 1
                    ins.then_inc(s_chain, 1)
                    dve.wait_ge(s_chain, chain[0])

                nc.vector.memset(bias1[:, :], 0.0)
                nc.vector.memset(gate_w[:, :], 0.0)
                nc.vector.memset(weights[:, :, :], 0.0).then_inc(s_zero, 1)

                def bounded(dst, neg, raw, size):
                    link(nc.vector.tensor_copy(dst, raw))
                    link(nc.vector.tensor_scalar(dst, dst, float(size - 1), float(-size), ALU.min, ALU.max))
                    link(nc.vector.tensor_scalar(neg, dst, 0.0, float(size), ALU.is_lt, ALU.mult))
                    return nc.vector.tensor_tensor(dst, dst, neg, ALU.add)

                dve.wait_ge(s_rows, 16)
                bounded(rows_f[:, :, :], rows_neg[:, :, :], raw_rows[:, :, :], PERSONS).then_inc(s_rows_ready, 1)
                dve.wait_ge(s_rowsT, 1)
                nc.vector.memset(person_idx[:, TILE_ROWS:], 0)
                nc.vector.tensor_copy(person_idx[:, 0:TILE_ROWS], members[:, 0, 0, 0:TILE_ROWS]).then_inc(s_idx, 1)
                dve.wait_ge(s_frows, 16)
                link(bounded(first_f[:, :], first_neg[:, :], raw_first[:, :], FIRSTS))
                nc.vector.tensor_copy(first_idx[:, :], first_f[:, :]).then_inc(s_fidx, 1)

                def step(n):
                    for q in range(STEP_QUADS):
                        slot, b0 = q // 2, QB * (q % 2)
                        if q % 2 == 0:
                            dve.wait_ge(s_ringed, 2 * n + slot + 1)
                        if not (is_first(n) and q < 2):
                            dve.wait_ge(s_tile, tiles_before(n, q - 1))
                        for c in range(CH):
                            here = members[:, slot, c, b0 * G:(b0 + QB) * G].rearrange("p (b i) -> p b i", i=G)
                            last = nc.vector.tensor_tensor(rows_of(q % 2, c, 1, ROWS_DVE),
                                                           repeated(here[:, :, 1:G], ROWS_DVE),
                                                           shifted(slot, c, b0, 1, ROWS_DVE), ALU.mult)
                        last.then_inc(s_edve, 1)

                steps(dve, step)

                def biggest(g0, g1):
                    link(nc.vector.tensor_reduce(out=stat[:, MAX, g0:g1], in_=all_gates[:, g0:g1, :], axis=AX.X, op=ALU.max))
                    nc.vector.tensor_scalar(stat[:, NMAX, g0:g1], stat[:, MAX, g0:g1], -1.0, None, ALU.mult).then_inc(s_max, 1)

                def pooled(g):
                    dve.wait_ge(s_exp, g + 1)
                    link(nc.vector.tensor_tensor_reduce(out=all_sums[:, g, :], in0=all_sums[:, g, :], in1=all_gates[:, g, :],
                                                        scale=1.0, scalar=0.0, op0=ALU.mult, op1=ALU.add,
                                                        accum_out=stat[:, NUM, g:g + 1]))

                dve.wait_ge(s_early, 32)
                biggest(0, FG - 1)
                dve.wait_ge(s_kept, 2 * STEPS)
                nc.vector.tensor_reduce(out=stat[:, FIRST, :], in_=first_vals[:, :].rearrange("p (g i) -> p g i", i=G),
                                        axis=AX.X, op=ALU.add)
                for g in range(FG - 1):
                    pooled(g)
                dve.wait_ge(s_late[0], 16)
                biggest(FG - 1, FG)
                dve.wait_ge(s_late[1], 16)
                pooled(FG - 1)
                link(nc.vector.reciprocal(stat[:, RDEN, :], stat[:, DEN, :]))
                link(nc.vector.tensor_tensor(stat[:, TOTAL, :], stat[:, NUM, :], stat[:, RDEN, :], ALU.mult))
                nc.vector.tensor_tensor(stat[:, TOTAL, :], stat[:, TOTAL, :], stat[:, FIRST, :], ALU.add).then_inc(s_fin, 1)
                dve.wait_ge(s_sigT, 1)
                nc.vector.tensor_scalar(result[:, :], score[0:FG, 0, 0:P], 2.0, -1.0, ALU.mult, ALU.add).then_inc(s_res, 1)

            @block.tensor
            def _(pe):
                pe.wait_ge(s_ident, 1)
                pe.wait_ge(s_rows_ready, 1)
                for h in range(2):
                    last = nc.tensor.transpose(members[:, 0, 0, h * IH:(h + 1) * IH], rows_f[:, h, :], ident[0:IH, 0:IH])
                last.then_inc(s_rowsT, 1)

                def transpose_oct(n, slot, rounds):
                    pe.wait_ge(s_gath[slot], 16 * GT * (rounds + 1))
                    if not (isinstance(rounds, int) and rounds == 0):
                        pe.wait_ge(s_edve, 4 * rounds - (0 if slot else 2))
                    for j in range(GT):
                        for c in range(CH):
                            last = nc.tensor.transpose(members[:, slot, c, j * P:(j + 1) * P],
                                                       gathered[:, slot, j, c * P:(c + 1) * P], ident[:, :])
                    last.then_inc(s_members, 1)

                pe.wait_ge(s_idx, 1)
                transpose_oct(0, 0, 0)
                pe.wait_ge(s_const, 16 * (2 * QB + 3))

                def step(n):
                    transpose_oct(n, 1, n)
                    for q in range(STEP_QUADS):
                        if q == 2 and not is_last(n):
                            transpose_oct(n + 1, 0, n + 1)
                        pe.wait_ge(s_edve, STEP_QUADS * n + q + 1)
                        pe.wait_ge(s_epool, STEP_QUADS * n + q + 1)
                        pe.wait_ge(s_eact, STEP_QUADS * n + q + 1)
                        for s in range(SEGS):
                            if not (is_first(n) and q == 0):
                                pe.wait_ge(s_read, tiles_before(n, q - 1) + s + 1 if q else TILES * n - SEGS + s + 1)
                            for c in range(CH):
                                for t in range(QB):
                                    last = nc.tensor.matmul(score[CT * t:CT * (t + 1), s, 0:SEG], weights[:, c, :],
                                                            pairs[:, q % 2, c, t, s * SEG:(s + 1) * SEG],
                                                            start=(c == 0), stop=(c == CH - 1))
                            last.then_inc(s_tile, 1)
                    for s in range(SEGS):
                        pe.wait_ge(s_read, TILES * n + SEGS * STEP_QUADS - SEGS + s + 1)
                        for q in range(STEP_QUADS):
                            last = nc.tensor.matmul(score[CT * q:CT * (q + 1), s, 0:SEG], gate_w[:, :],
                                                    hidden[:, q, s * SEG:(s + 1) * SEG], start=True, stop=True)
                        last.then_inc(s_tile, 1)

                steps(pe, step)
                pe.wait_ge(s_sig, 1)
                nc.tensor.transpose(score[0:FG, 0, 0:P], stat[:, SIG, :], ident[:, :]).then_inc(s_sigT, 1)

            @block.scalar
            def _(act):
                def next_persons(slot, o):
                    return nc.scalar.copy(near_persons[:, slot, :], person_idx[:, bass.ds(GT * o, GT)])

                def keep_firsts(slot, o, rounds):
                    act.wait_ge(s_first[slot], 16 * GT * rounds)
                    nc.scalar.copy(first_vals[:, bass.ds(GT * o, GT)], first_now[:, slot, :]).then_inc(s_kept, 1)

                def ring_oct(slot, o, rounds):
                    start = isinstance(rounds, int) and rounds == 0
                    if not start:
                        keep_firsts(slot, o - 2, rounds)
                    nc.scalar.copy(near_firsts[:, slot, :], first_idx[:, bass.ds(GT * o, GT)])
                    act.wait_ge(s_members, o + 1)
                    if not (slot == 1 and is_last(rounds)):
                        next_persons(slot, o + 2)
                    if not start:
                        act.wait_ge(s_edve, 2 * (o - 1))
                        act.wait_ge(s_epool, 2 * (o - 1))
                    for c in range(CH):
                        here = members[:, slot, c, 0:OB * G].rearrange("p (b i) -> p b i", i=G)
                        nc.scalar.copy(ringed[:, slot, c, :, 0:G], here)
                        last = nc.scalar.copy(ringed[:, slot, c, :, G:RING], here[:, :, 1:1 + ROWS])
                    last.then_inc(s_ringed, 1)

                def zero_row(slot, b0, quad_slot):
                    for c in range(CH):
                        for t in range(QB):
                            last = nc.scalar.activation(pairs[:, quad_slot, c, t, ROWS * ROW:PAIRS],
                                                        ringed[:, slot, c, b0 + t, 1:G], ACT.Copy,
                                                        scale=ringed[:, slot, c, b0 + t, 0:1])
                    last.then_inc(s_eact, 1)

                act.wait_ge(s_idx, 1)
                next_persons(0, 0)
                next_persons(1, 1).then_inc(s_near, 1)
                act.wait_ge(s_fidx, 1)
                ring_oct(0, 0, 0)
                act.wait_ge(s_ringed, 1)
                for q in range(2):
                    zero_row(0, QB * q, q)
                act.wait_ge(s_const, 16 * (2 * QB + 3))

                def step(n):
                    ring_oct(1, 2 * n + 1, n)
                    for q in range(STEP_QUADS):
                        if q == 2 and not is_last(n):
                            ring_oct(0, 2 * n + 2, n + 1)
                        if not (is_first(n) and q < 2):
                            act.wait_ge(s_sumout[q % 2], 32 * n + 16 * (q // 2))
                        for s in range(SEGS):
                            act.wait_ge(s_tile, tiles_before(n, q) + s + 1)
                            seg = slice(s * SEG, (s + 1) * SEG)
                            nc.scalar.activation(hidden[:, q, seg], score[:, s, 0:SEG], ACT.Sigmoid, bias=bias1[:, :])
                            nc.scalar.copy(sums[:, q % 2, seg], score[:, s, 0:SEG]).then_inc(s_read, 1)
                        if not (is_last(n) and q >= 2):
                            later = (q + 2) // 2
                            act.wait_ge(s_ringed, 2 * n + later + 1)
                            zero_row(later % 2, QB * (q % 2), q % 2)
                    if not is_first(n):
                        act.wait_ge(s_gateout, 16 * n)
                    for s in range(SEGS):
                        act.wait_ge(s_tile, TILES * n + SEGS * STEP_QUADS + s + 1)
                        nc.scalar.activation(gates[:, s * SEG:(s + 1) * SEG], score[:, s, 0:SEG], ACT.Sigmoid,
                                             bias=bias2[:, :]).then_inc(s_read, 1)

                steps(act, step)
                for slot in range(2):
                    keep_firsts(slot, 2 * STEPS - 2 + slot, STEPS)
                for g in range(FG):
                    act.wait_ge(s_max, 1 if g < FG - 1 else 2)
                    nc.scalar.activation(all_gates[:, g, :], all_gates[:, g, :], ACT.Exp, bias=stat[:, NMAX, g:g + 1],
                                         accum_out=stat[:, DEN, g:g + 1]).then_inc(s_exp, 1)
                act.wait_ge(s_fin, 1)
                nc.scalar.activation(stat[:, SIG, :], stat[:, TOTAL, :], ACT.Sigmoid).then_inc(s_sig, 1)


_INS = ['r_group', 'L0_rec_person_embed', 'L0_rec_first_embed', 'L0_rec_p', 'L0_rec_W1', 'L0_rec_b1', 'L0_rec_W2', 'L0_rec_b2']


def kernel(**inputs):
    import numpy as _np
    import concourse.bacc as _bacc
    from concourse import mybir as _mybir
    from concourse.bass_utils import run_bass_kernel_spmd as _run

    nc = _bacc.Bacc("TRN2", target_bir_lowering=False, num_devices=1)
    arrays, args = {}, []
    for name in _INS:
        a = _np.ascontiguousarray(inputs[name])
        arrays[f"in_{name}_dram"] = a
        args.append(nc.dram_tensor(f"in_{name}_dram", a.shape, _mybir.dt.from_np(a.dtype), kind="ExternalInput").ap())
    groups, members = inputs['r_group'].shape
    scratch = (groups, members * (members - 1) // 2)
    for name in ("sum_rows", "gate_rows"):
        args.append(nc.dram_tensor(name, scratch, _mybir.dt.float32, kind="Internal").ap())
    args.append(nc.dram_tensor("out_0_dram", (groups,), _mybir.dt.float32, kind="ExternalOutput").ap())
    group_scores_program(nc, *args)
    r = _run(nc, [arrays], core_ids=[0])
    return r.results[0]["out_0_dram"]
```
